# Optimizing a Trainium2 kernel written in Bass

```python
import numpy as np
import jax
import jax.numpy as jnp

def _softmax(x, axis=-1):
    return jax.nn.softmax(x, axis=axis)

def _gelu(x):
    return jax.nn.gelu(x, approximate=True)

def _silu(x):
    return jax.nn.silu(x)

def _sigmoid(x):
    return jax.nn.sigmoid(x)

def _layernorm(x, axis=-1, eps=1e-05):
    m = jnp.mean(x, axis=axis, keepdims=True)
    v = jnp.var(x, axis=axis, keepdims=True)
    return (x - m) / jnp.sqrt(v + eps)

def _scatter_add(tgt, idx, src, axis=0):
    return tgt.at[idx].add(src)

def _segment_sum(src, seg, n):
    return jax.ops.segment_sum(src, seg, n)
kernel_name = 'mk_vit_tower_d1_tok_img1024_r4_0a0df3'

def setup_inputs(seed: int=0):
    np.random.seed(seed)
    _w = jnp.asarray

    def _rec_inputs():
        import jax
        import jax.numpy as jnp
        _rk = jax.random.key(seed)
        x = -0.00016672 + 0.999947 * jax.random.normal(jax.random.fold_in(_rk, 1), (32, 3, 96, 96), jnp.float32)
        return x
    x = _rec_inputs()

    def _L0_tok_setup():
        import jax, jax.numpy as jnp
        import numpy as np
        IMG = 96
        PATCH = 16
        C_IN = 3
        EMBED = 256
        NPH = IMG // PATCH
        NUM_PATCHES = NPH * NPH
        PATCH_DIM = PATCH * PATCH * C_IN
        key = jax.random.key(seed)
        k_x, k_w, k_b, k_cls, k_pos = jax.random.split(key, 5)
        x = jax.random.normal(k_x, (64, C_IN, IMG, IMG), dtype=jnp.float32)
        W = jax.random.normal(k_w, (EMBED, PATCH_DIM), dtype=jnp.float32) * (1.0 / np.sqrt(PATCH_DIM))
        b = jax.random.normal(k_b, (EMBED,), dtype=jnp.float32) * 0.01
        cls_token = jax.random.normal(k_cls, (1, 1, EMBED), dtype=jnp.float32) * 0.02
        pos_embed = jax.random.normal(k_pos, (1, NUM_PATCHES + 1, EMBED), dtype=jnp.float32) * 0.02
        return {'x': x, 'W': W, 'b': b, 'cls_token': cls_token, 'pos_embed': pos_embed}
    _L0_tok_all = _L0_tok_setup()
    _L0_tok_in = {k: v for k, v in _L0_tok_all.items() if k in ('W', 'b', 'cls_token', 'pos_embed')}
    del _L0_tok_all

    def _L0_attn_setup():
        import jax, jax.numpy as jnp
        import numpy as np
        D_MODEL = 256
        NUM_HEADS = 16
        HEAD_DIM = D_MODEL // NUM_HEADS
        LN_EPS = 1e-05

        def _layernorm(x, gamma, beta):
            mu = jnp.mean(x, axis=-1, keepdims=True)
            var = jnp.mean(jnp.square(x - mu), axis=-1, keepdims=True)
            return (x - mu) * jax.lax.rsqrt(var + LN_EPS) * gamma + beta
        key = jax.random.key(seed)
        ks = jax.random.split(key, 7)
        B, S, D = (2, 512, D_MODEL)
        x = jax.random.normal(ks[0], (B, S, D), dtype=jnp.float32)
        lim1 = 1.0 / np.sqrt(D)
        W1 = jax.random.uniform(ks[1], (D, 4 * D), minval=-lim1, maxval=lim1, dtype=jnp.float32)
        b1 = jax.random.uniform(ks[2], (4 * D,), minval=-lim1, maxval=lim1, dtype=jnp.float32)
        W2 = jax.random.uniform(ks[3], (D, D), minval=-lim1, maxval=lim1, dtype=jnp.float32)
        b2 = jax.random.uniform(ks[4], (D,), minval=-lim1, maxval=lim1, dtype=jnp.float32)
        gamma = jnp.ones((D,), dtype=jnp.float32)
        beta = jnp.zeros((D,), dtype=jnp.float32)
        return {'x': x, 'W1': W1, 'b1': b1, 'W2': W2, 'b2': b2, 'gamma': gamma, 'beta': beta}
    _L0_attn_all = _L0_attn_setup()
    _L0_attn_in = {k: v for k, v in _L0_attn_all.items() if k in ('W1', 'b1', 'W2', 'b2', 'gamma', 'beta')}
    del _L0_attn_all

    def _L0_ffn_setup():
        import jax, jax.numpy as jnp
        import numpy as np
        B, T, D, F, E, TOP_K = (2, 512, 256, 1024, 8, 2)
        INIT = 0.02
        key = jax.random.key(seed)
        k0, k1, k2, k3, k4 = jax.random.split(key, 5)
        x = jax.random.normal(k0, (B, T, D), dtype=jnp.float32)
        Wg = jax.random.normal(k1, (D, E), dtype=jnp.float32) * INIT
        W1 = jax.random.normal(k2, (E, D, F), dtype=jnp.float32) * INIT
        W3 = jax.random.normal(k3, (E, D, F), dtype=jnp.float32) * INIT
        W2 = jax.random.normal(k4, (E, F, D), dtype=jnp.float32) * INIT
        return {'x': x, 'Wg': Wg, 'W1': W1, 'W3': W3, 'W2': W2}
    _L0_ffn_all = _L0_ffn_setup()
    _L0_ffn_in = {k: v for k, v in _L0_ffn_all.items() if k in ('Wg', 'W1', 'W3', 'W2')}
    del _L0_ffn_all
    return {'x': x, 'L0_tok_W': _L0_tok_in['W'], 'L0_tok_b': _L0_tok_in['b'], 'L0_tok_cls_token': _L0_tok_in['cls_token'], 'L0_tok_pos_embed': _L0_tok_in['pos_embed'], 'L0_attn_W1': _L0_attn_in['W1'], 'L0_attn_b1': _L0_attn_in['b1'], 'L0_attn_W2': _L0_attn_in['W2'], 'L0_attn_b2': _L0_attn_in['b2'], 'L0_attn_gamma': _L0_attn_in['gamma'], 'L0_attn_beta': _L0_attn_in['beta'], 'L0_ffn_Wg': _L0_ffn_in['Wg'], 'L0_ffn_W1': _L0_ffn_in['W1'], 'L0_ffn_W3': _L0_ffn_in['W3'], 'L0_ffn_W2': _L0_ffn_in['W2']}

def reference(x, L0_tok_W, L0_tok_b, L0_tok_cls_token, L0_tok_pos_embed, L0_attn_W1, L0_attn_b1, L0_attn_W2, L0_attn_b2, L0_attn_gamma, L0_attn_beta, L0_ffn_Wg, L0_ffn_W1, L0_ffn_W3, L0_ffn_W2):
    import jax
    import jax.numpy as jnp

    def _L0_tok_ref(x, W, b, cls_token, pos_embed):
        import jax, jax.numpy as jnp
        import numpy as np
        IMG = 96
        PATCH = 16
        C_IN = 3
        EMBED = 256
        NPH = IMG // PATCH
        NUM_PATCHES = NPH * NPH
        PATCH_DIM = PATCH * PATCH * C_IN
        B, C, H, Wd = x.shape
        nph, npw = (H // PATCH, Wd // PATCH)
        patches = x.reshape(B, C, nph, PATCH, npw, PATCH)
        patches = patches.transpose(0, 2, 4, 1, 3, 5)
        patches = patches.reshape(B, nph * npw, C * PATCH * PATCH)
        proj = jnp.einsum('bnd,ed->bne', patches, W) + b
        cls = jnp.broadcast_to(cls_token, (B, 1, cls_token.shape[-1]))
        out = jnp.concatenate([cls, proj], axis=1) + pos_embed
        return out

    def _L0_attn_ref(x, W1, b1, W2, b2, gamma, beta):
        import jax, jax.numpy as jnp
        import numpy as np
        D_MODEL = 256
        NUM_HEADS = 16
        HEAD_DIM = D_MODEL // NUM_HEADS
        LN_EPS = 1e-05

        def _layernorm(x, gamma, beta):
            mu = jnp.mean(x, axis=-1, keepdims=True)
            var = jnp.mean(jnp.square(x - mu), axis=-1, keepdims=True)
            return (x - mu) * jax.lax.rsqrt(var + LN_EPS) * gamma + beta
        B, S, D = x.shape
        H, Dh = (NUM_HEADS, HEAD_DIM)
        x_proj = jax.nn.silu(x @ W1 + b1)
        u, v, q, k = jnp.split(x_proj, 4, axis=-1)
        qh = q.reshape(B, S, H, Dh)
        kh = k.reshape(B, S, H, Dh)
        vh = v.reshape(B, S, H, Dh)
        scores = jnp.einsum('bqhd,bkhd->bhqk', qh, kh)
        attn = jax.nn.silu(scores) / S
        av = jnp.einsum('bhqk,bkhd->bqhd', attn, vh).reshape(B, S, D)
        y = _layernorm(av * u, gamma, beta) @ W2 + b2
        return y

    def _L0_ffn_ref(x, Wg, W1, W3, W2):
        import jax, jax.numpy as jnp
        import numpy as np
        B, T, D, F, E, TOP_K = (2, 512, 256, 1024, 8, 2)
        INIT = 0.02
        Bb, Tt, Dd = x.shape
        xf = x.reshape(-1, Dd)
        logits = xf @ Wg
        top_v, top_i = jax.lax.top_k(logits, TOP_K)
        top_w = jax.nn.softmax(top_v, axis=-1)
        h1 = jnp.einsum('nd,edf->enf', xf, W1)
        h3 = jnp.einsum('nd,edf->enf', xf, W3)
        y = jnp.einsum('enf,efd->end', jax.nn.silu(h1) * h3, W2)
        y = jnp.transpose(y, (1, 0, 2))
        sel = jnp.take_along_axis(y, top_i[:, :, None], axis=1)
        out = jnp.sum(sel * top_w[:, :, None], axis=1)
        return out.reshape(Bb, Tt, Dd)
    h = _L0_tok_ref(x, L0_tok_W, L0_tok_b, L0_tok_cls_token, L0_tok_pos_embed)
    h = h + _L0_attn_ref(_layernorm(h, axis=-1), L0_attn_W1, L0_attn_b1, L0_attn_W2, L0_attn_b2, L0_attn_gamma, L0_attn_beta)
    h = h + _L0_ffn_ref(_layernorm(h, axis=-1), L0_ffn_Wg, L0_ffn_W1, L0_ffn_W3, L0_ffn_W2)
    return h

_drawn_inputs = setup_inputs


def setup_inputs(seed=0):
    import zlib

    import numpy as np

    out = dict(_drawn_inputs(seed))
    spreads = {'L0_attn_gamma': (1.0, 0.2), 'L0_attn_beta': (0.0, 0.1)}
    factors = {'L0_tok_b': 3.646, 'L0_ffn_Wg': 8.439}
    for name, (base, spread) in spreads.items():
        noise = np.random.default_rng([zlib.crc32(name.encode()), seed]).standard_normal(out[name].shape)
        drawn = base * np.exp(spread * noise) if base else spread * noise
        out[name] = jnp.asarray(drawn.astype(out[name].dtype))
    for name, factor in factors.items():
        out[name] = (out[name] * factor).astype(out[name].dtype)
    return out
```

```python
import concourse.bass as bass
from concourse import mybir
from contextlib import ExitStack

B, C, IMG, PATCH = 32, 3, 96, 16
D = 256
NPH = IMG // PATCH
S = NPH * NPH + 1
N = B * S
P = 128
NT = -(-N // P)
NP = NT * P
LAST = N - (NT - 1) * P
PD = C * PATCH * PATCH
KC = PD // P
NPOS = S + 2
DC = D // P
H, DH = 16, 16
HH = P // DH
GB = 3
NG = -(-B // GB)
GT = GB * S
F, E = 1024, 8
EPS = 1e-5
CAP = N + P
TILES = (2 * N + E * (P - 1)) // P
ROW = D + 4
XROWS = E * CAP + P
RING = 3
W1C, W3C, W2C = DC * F, DC * F, (F // P) * D
WCOLS = W1C + W3C + W2C


def vit_block_kernel(nc, xpatch, onehot, wemb, wpos, w1, b1f, b1v, w2, b2, gamma, beta, wg, experts,
                     headmask, c8, ctile, cslot, tokid, tri, padrow, out):
    f32, i32 = mybir.dt.float32, mybir.dt.int32
    ALU, ACT, AX = mybir.AluOpType, mybir.ActivationFunctionType, mybir.AxisListType.X
    ds = bass.ds

    v_dram = nc.dram_tensor("v_dram", [NP, D], f32, kind="Internal").ap()
    rows_dram = nc.dram_tensor("rows_dram", [XROWS, ROW], f32, kind="Internal").ap()

    ctx = ExitStack()
    with ctx:
        def sb(name, shape, dt=f32):
            return ctx.enter_context(nc.sbuf_tensor(name, shape, dt))

        def sem(name):
            return ctx.enter_context(nc.semaphore(name))

        ring = sb("ring", [P, RING, WCOLS])
        wemb_sb = sb("wemb_sb", [P, KC, D])
        wpos_sb = sb("wpos_sb", [NPOS, D])
        w1_sb = sb("w1_sb", [P, DC, 4 * D])
        w2_sb = sb("w2_sb", [P, DC, D])
        wg_sb = sb("wg_sb", [P, DC, E])
        b1f_sb = sb("b1f_sb", [P, 6])
        b1v_sb = sb("b1v_sb", [1, D])
        b2_sb = sb("b2_sb", [1, D])
        gamma_sb = sb("gamma_sb", [P, DC])
        beta_sb = sb("beta_sb", [P, DC])
        mask_sb = sb("mask_sb", [P, HH])
        c8_sb = sb("c8_sb", [P, 2, E])
        ctile_sb = sb("ctile_sb", [P, TILES])
        cslot_sb = sb("cslot_sb", [P, NT])
        tokid_sb = sb("tokid_sb", [P, 2, NT])
        tri_sb = sb("tri_sb", [P, P])
        padrow_sb = sb("padrow_sb", [P, ROW])
        ident = sb("ident", [P, P])
        ones = sb("ones", [P, P])
        eps_sb = sb("eps_sb", [P, 1])

        xb = [sb(f"xb{i}", [P, KC, P]) for i in range(2)]
        pb = [sb(f"pb{i}", [NPOS, P]) for i in range(2)]
        h_all = sb("h_all", [P, NT, D])
        stats = sb("stats", [P, 3, NT, 6])
        mv = sb("mv", [P, 3, NT, 2])
        rstd = sb("rstd", [P, 3, 2, NT])
        xn = [sb(f"xn{i}", [P, D]) for i in range(2)]
        xT = sb("xT", [P, DC, 2 * P])
        uT = sb("uT", [P, DC, NP])
        qT = sb("qT", [P, DC, NP])
        kT = sb("kT", [P, DC, NP])
        v_sb = [sb(f"v_sb{i}", [P, D]) for i in range(2)]
        qblk = [sb(f"qblk{i}", [P, GB, HH, S]) for i in range(2)]
        kz = [sb(f"kz{i}", [P, GB * (GT + S)]) for i in range(2)]
        vz = [sb(f"vz{i}", [P, GB, P]) for i in range(2)]
        at = [sb(f"at{i}", [GT, HH * S]) for i in range(2)]
        yT = sb("yT", [P, DC, NP])
        ycur = [sb(f"ycur{i}", [P, DC, P]) for i in range(2)]
        y_nat = qT[:, :, :].rearrange("p c n -> p (c n)").rearrange("p (t d) -> p t d", d=D)
        zT = [sb(f"zT{i}", [P, DC, P]) for i in range(2)]
        rows = sb("rows", [P, NT, ROW])
        lg = sb("lg", [P, NT, E])
        r8 = sb("r8", [P, 10, NT, E])
        r1 = sb("r1", [P, 10, NT])
        e8 = sb("e8", [P, 8, E])
        slot_i = sb("slot_i", [P, 2, NT], i32)
        te = sb("te", [P, 2, TILES, E])
        t1 = sb("t1", [P, 10, TILES])
        tile_i = sb("tile_i", [P, 3, TILES], i32)
        exp_i = sb("exp_i", [P, 2, E], i32)
        xg = [sb(f"xg{i}", [P, ROW]) for i in range(2)]
        ysb = [sb(f"ysb{i}", [P, D]) for i in range(2)]
        tok_i = [sb(f"tok_i{i}", [P, 1], i32) for i in range(2)]
        wt = [sb(f"wt{i}", [P, 2]) for i in range(2)]
        xTs = zT
        act_t = uT[:, 0, 0:F]
        g = [qT[:, 0, 0:F], qT[:, 1, 0:F]]
        gT = kT[:, 0, 0:F].rearrange("p (j t) -> p j t", t=P)

        bank = [ctx.enter_context(nc.psum_tensor(f"bank{i}", [P, 512], f32)) for i in range(2)]
        av_ps = [ctx.enter_context(nc.psum_tensor(f"av{i}", [P, 3, 512], f32)) for i in range(2)]
        ps = [bank[0][:, :], bank[1][:, :]] + [av_ps[i][:, j, :] for i in range(2) for j in range(3)]

        embed_w_in = sem("embed_w_in")
        const_in = sem("const_in")
        x_in = [sem(f"x_in{i}") for i in range(2)]
        w_in = sem("w_in")
        vz_in = [sem(f"vz_in{i}") for i in range(2)]
        v_out = [sem(f"v_out{i}") for i in range(2)]
        pads_out = sem("pads_out")
        rows_out = sem("rows_out")
        h2_out = sem("h2_out")
        row_in = [sem(f"row_in{i}") for i in range(2)]
        added = sem("added")
        ident_set, ident_ready, zeros_ready = sem("ident_set"), sem("ident_ready"), sem("zeros_ready")
        vz_zero, kz_zero = sem("vz_zero"), sem("kz_zero")
        embed_mm, h_ready, stat1 = sem("embed_mm"), sem("h_ready"), sem("stat1")
        mv_ready = [sem(f"mv_ready{i}") for i in range(3)]
        std_ready = [sem(f"std_ready{i}") for i in range(3)]
        xn_ready, xt_mm, xt_ready, proj_mm, v_mm = (sem("xn_ready"), sem("xt_mm"), sem("xt_ready"),
                                                    sem("proj_mm"), sem("v_mm"))
        uqk_ready, v_ready = sem("uqk_ready"), sem("v_ready")
        qblk_ready, kz_ready, score_mm, at_ready, av_mm, y_done = (
            sem("qblk_ready"), sem("kz_ready"), sem("score_mm"), sem("at_ready"), sem("av_mm"), sem("y_done"))
        ycur_ready, yt_mm, ynat_ready, stat2 = sem("ycur_ready"), sem("yt_mm"), sem("ynat_ready"), sem("stat2")
        z_ready, zt_mm, zt_ready, out_mm, h2_ready = (sem("z_ready"), sem("zt_mm"), sem("zt_ready"),
                                                      sem("out_mm"), sem("h2_ready"))
        hn_ready, row_ready, hnt_mm, hnt_ready, lg_mm, lg_ready = (
            sem("hn_ready"), sem("row_ready"), sem("hnt_mm"), sem("hnt_ready"), sem("lg_mm"), sem("lg_ready"))
        gap_ready, expw_ready, sel_ready, rank_mm = (sem("gap_ready"), sem("expw_ready"), sem("sel_ready"),
                                                     sem("rank_mm"))
        slots_ready, tables_ready = sem("slots_ready"), sem("tables_ready")
        tx_mm, tx_ready, up_mm, silu_ready, g_ready = (sem("tx_mm"), sem("tx_ready"), sem("up_mm"),
                                                       sem("silu_ready"), sem("g_ready"))
        gt_mm, gt_a, gt_b, tile_mm, y_ready, meta_ready = (sem("gt_mm"), sem("gt_a"), sem("gt_b"),
                                                           sem("tile_mm"), sem("y_ready"), sem("meta_ready"))
        dve_step, odd_done = sem("dve_step"), sem("odd_done")

        CONSTS = [
            (w1_sb[:, :, :], w1), (b1f_sb[:, :], b1f), (b1v_sb[:, :], b1v), (mask_sb[:, :], headmask),
            (w2_sb[:, :, :], w2), (b2_sb[:, :], b2), (gamma_sb[:, :], gamma), (beta_sb[:, :], beta),
            (wg_sb[:, :, :], wg), (c8_sb[:, :, :], c8), (ctile_sb[:, :], ctile), (cslot_sb[:, :], cslot),
            (tokid_sb[:, :, :], tokid), (tri_sb[:, :], tri), (padrow_sb[:, :], padrow),
        ]
        ALL_CONST = 16 * len(CONSTS)

        block = ctx.enter_context(nc.Block())

        @block.sync
        def _(sp):
            sp.dma_start(wemb_sb[:, :, :], wemb).then_inc(embed_w_in, 16)
            sp.dma_start(wpos_sb[:, :], wpos).then_inc(embed_w_in, 16)

            def load_x(p, t):
                sp.dma_start(xb[p][:, :, :], xpatch[t]).then_inc(x_in[p], 16)
                sp.dma_start(pb[p][:, :], onehot[t]).then_inc(x_in[p], 16)

            load_x(0, 0)
            load_x(1, 1)
            for dst, src in CONSTS:
                sp.dma_start(dst, src).then_inc(const_in, 16)
            for r in range(RING):
                sp.dma_start(ring[:, r, :], experts[r]).then_inc(w_in, 16)
            with sp.Fori(1, NT // 2) as it:
                for p in range(2):
                    sp.wait_ge(embed_mm, it * 2 + (p - 1))
                    sp.dma_start(xb[p][:, :, :], xpatch[ds(it * 2 + p, 1)]).then_inc(x_in[p], 16)
                    sp.dma_start(pb[p][:, :], onehot[ds(it * 2 + p, 1)]).then_inc(x_in[p], 16)
            with sp.Fori(0, NT // 2) as it:
                for p in range(2):
                    sp.wait_ge(v_ready, it * 2 + (p + 1))
                    sp.dma_start(v_dram[ds(it * 2 * P + p * P, P), :], v_sb[p][:, :]).then_inc(v_out[p], 16)
            sp.wait_ge(vz_zero, 2)
            for p in range(2):
                sp.wait_ge(v_out[p], 16 * (NT // 2))

            def load_v(g_, half):
                for b in range(GB):
                    sp.dma_start(vz[half][b * S:(b + 1) * S, b, :],
                                 v_dram[ds(g_ * GT + b * S, S), half * P:(half + 1) * P]).then_inc(vz_in[half], 16)

            load_v(0, 0)
            load_v(0, 1)
            with sp.Fori(1, NG) as gi:
                for half in range(2):
                    sp.wait_ge(av_mm, gi * 2 + (half - 1))
                    load_v(gi, half)
            sp.wait_ge(h2_ready, NT)
            sp.dma_start(out[0:(NT - 1) * P, :].rearrange("(t p) d -> p t d", p=P),
                         h_all[:, 0:NT - 1, :]).then_inc(h2_out, 16)
            sp.dma_start(out[(NT - 1) * P:N, :], h_all[0:LAST, NT - 1, :]).then_inc(h2_out, 16)
            sp.dma_start(out[N:N + P, :], padrow_sb[:, 0:D]).then_inc(h2_out, 16)
            sp.dma_start(rows_dram[E * CAP:XROWS, :], padrow_sb[:, :]).then_inc(pads_out, 16)
            sp.wait_ge(tables_ready, 1)
            for e in range(E):
                r = sp.value_load(exp_i[0:1, 0, e:e + 1], min_val=e * CAP, max_val=e * CAP + N)
                sp.dma_start(rows_dram[ds(r, P), :], padrow_sb[:, :]).then_inc(pads_out, 16)
            sp.wait_ge(w_in, 16 * RING)
            for e in range(RING, E):
                r = sp.value_load(exp_i[0:1, 1, e - RING:e - RING + 1], min_val=1, max_val=TILES + 1)
                sp.wait_ge(tile_mm, r)
                sp.dma_start(ring[:, e % RING, :], experts[e]).then_inc(w_in, 16)
                sp.wait_ge(w_in, 16 * (e + 1))
            sp.wait_ge(pads_out, 16 * (E + 1))
            sp.wait_ge(added, 16 * TILES)

        @block.gpsimd
        def _(pool):
            nc.gpsimd.memset(ident[:, :], 0.0).then_inc(ident_set, 1)
            pool.wait_ge(ident_set, 1)
            nc.gpsimd.affine_select(out=ident[:, :], in_=ident[:, :], compare_op=ALU.not_equal, fill=1.0, base=0,
                                    pattern=[[-1, P]], channel_multiplier=1).then_inc(ident_ready, 1)
            for half in range(2):
                nc.gpsimd.memset(kz[half][:, :], 0.0).then_inc(kz_zero, 1)
                nc.gpsimd.memset(vz[half][:, :, :], 0.0).then_inc(vz_zero, 1)
            pool.wait_ge(kz_zero, 2)
            pool.wait_ge(uqk_ready, 6 * (NT // 2))

            def spread_k(g_, half):
                dst = kz[half][:, :].rearrange("p (b c) -> p b c", b=GB)[:, :, 0:S]
                src = kT[:, half, ds(g_ * GT, GT)].rearrange("p (b s) -> p b s", b=GB)
                nc.gpsimd.tensor_copy(dst, src).then_inc(kz_ready, 1)

            spread_k(0, 0)
            spread_k(0, 1)
            with pool.Fori(1, NG) as gi:
                for half in range(2):
                    pool.wait_ge(score_mm, gi * 2 + (half - 1))
                    spread_k(gi, half)
            pool.wait_ge(row_ready, NT)
            pool.wait_ge(slots_ready, 1)
            for c in range(2):
                for t in range(NT):
                    n = P if t < NT - 1 else LAST
                    nc.gpsimd.indirect_dma_start(
                        rows_dram[:, :], bass.IndirectOffsetOnAxis(ap=slot_i[0:n, c, t:t + 1], axis=0),
                        rows[0:n, t, :], None).then_inc(rows_out, 16)
            pool.wait_ge(rows_out, 16 * 2 * NT)

            def add_tile(t, p, first=False):
                pool.wait_ge(y_ready, t + 1)
                if not first:
                    pool.wait_ge(added, t * 16)
                pool.wait_ge(h2_out, 48)
                nc.gpsimd.indirect_dma_start(
                    out[:, :], bass.IndirectOffsetOnAxis(ap=tok_i[p][:, 0:1], axis=0), ysb[p][:, :], None,
                    compute_op=ALU.add).then_inc(added, 16)

            for t in range(TILES):
                add_tile(t, t % 2, first=(t == 0))

        @block.scalar
        def _(act):
            def store_h(t, p):
                act.wait_ge(embed_mm, t + 1)
                nc.scalar.activation(h_all[:, ds(t, 1), :], ps[p][:, 0:D].rearrange("p (a d) -> p a d", a=1),
                                     ACT.Copy).then_inc(h_ready, 1)

            with act.Fori(0, NT // 2) as it:
                for p in range(2):
                    store_h(it * 2 + p, p)

            def root(k):
                act.wait_ge(mv_ready[k], NT)
                nc.scalar.activation(rstd[:, k, 0, :], mv[:, k, :, 1], ACT.Sqrt,
                                     bias=eps_sb[:, 0:1]).then_inc(std_ready[k], 1)

            act.wait_ge(zeros_ready, 1)
            root(0)
            act.wait_ge(const_in, ALL_CONST)

            def project(it, first):
                for p in range(2):
                    act.wait_ge(xt_mm, it * 2 + (p + 1))
                    if not first and p == 0:
                        act.wait_ge(v_mm, it * 2)
                    nc.scalar.activation(xT[:, :, p * P:(p + 1) * P],
                                         ps[p][:, 0:D].rearrange("p (c t) -> p c t", c=DC),
                                         ACT.Copy).then_inc(xt_ready, 1)
                for f, dst in enumerate((uT, uT, qT, qT, kT, kT)):
                    act.wait_ge(proj_mm, it * 6 + (2 * (f // 2) + 2))
                    nc.scalar.activation(dst[:, f % 2, ds(it * 2 * P, 2 * P)],
                                         ps[2 + f // 2][:, (f % 2) * 256:(f % 2) * 256 + 256], ACT.Silu,
                                         bias=b1f_sb[:, f:f + 1]).then_inc(uqk_ready, 1)
                for p in range(2):
                    act.wait_ge(v_mm, it * 2 + 2)
                    if not first:
                        act.wait_ge(v_out[p], it * 16)
                    nc.scalar.activation(v_sb[p][:, :], ps[5][:, p * 256:p * 256 + 256],
                                         ACT.Silu).then_inc(v_ready, 1)

            project(0, True)
            with act.Fori(1, NT // 2) as it:
                project(it, False)

            def silu_scores(g_, half, first):
                act.wait_ge(score_mm, g_ * 2 + (half + 1))
                if not first:
                    act.wait_ge(av_mm, g_ * 2 + (half - 1))
                nc.scalar.activation(at[half][:, :], ps[half][0:GT, 0:HH * S], ACT.Silu).then_inc(at_ready, 1)

            for half in range(2):
                silu_scores(0, half, True)
            with act.Fori(1, NG) as gi:
                for half in range(2):
                    silu_scores(gi, half, False)

            act.wait_ge(y_done, 2 * NG)

            def y_cur(it, p, first):
                if not first:
                    act.wait_ge(yt_mm, it * 2 + (p - 1))
                nc.scalar.activation(ycur[p][:, :, :], yT[:, :, ds(it * 2 * P + p * P, P)],
                                     ACT.Copy).then_inc(ycur_ready, 1)

            def y_store(it, p):
                act.wait_ge(yt_mm, it * 2 + (p + 1))
                nc.scalar.activation(y_nat[:, ds(it * 2 + p, 1), :],
                                     ps[p][:, 0:D].rearrange("p (a d) -> p a d", a=1),
                                     ACT.Copy).then_inc(ynat_ready, 1)

            for p in range(2):
                y_cur(0, p, True)
            with act.Fori(1, NT // 2) as it:
                for p in range(2):
                    y_store(it - 1, p)
                for p in range(2):
                    y_cur(it, p, False)
            for p in range(2):
                y_store(NT // 2 - 1, p)
            root(1)

            def scale_z(it, p):
                act.wait_ge(zt_mm, it * 2 + (p + 1))
                for c in range(DC):
                    last = nc.scalar.activation(zT[p][:, c, :], ps[p][:, c * P:(c + 1) * P], ACT.Identity,
                                                scale=gamma_sb[:, c:c + 1], bias=beta_sb[:, c:c + 1])
                last.then_inc(zt_ready, 1)

            for p in range(2):
                scale_z(0, p)
            with act.Fori(1, NT // 2) as it:
                for p in range(2):
                    act.wait_ge(out_mm, it * 2 + (p - 1))
                    scale_z(it, p)
            root(2)

            def route_rows(it, p, first):
                act.wait_ge(hn_ready, it * 2 + (p + 1))
                nc.scalar.activation(rows[:, ds(it * 2 + p, 1), 0:D],
                                     xn[p][:, :].rearrange("p (a d) -> p a d", a=1), ACT.Copy).then_inc(row_ready, 1)
                act.wait_ge(hnt_mm, it * 2 + (p + 1))
                if not first:
                    act.wait_ge(lg_mm, it * 2 + (p - 1))
                nc.scalar.activation(zT[p][:, :, :], ps[p][:, 0:D].rearrange("p (c t) -> p c t", c=DC),
                                     ACT.Copy).then_inc(hnt_ready, 1)

            act.wait_ge(out_mm, NT)
            for p in range(2):
                route_rows(0, p, True)
            with act.Fori(1, NT // 2) as it:
                for p in range(2):
                    route_rows(it, p, False)
            act.wait_ge(gap_ready, 1)
            nc.scalar.activation(r1[:, 4, :], r1[:, 3, :], ACT.Exp).then_inc(expw_ready, 1)

            def load_rows(t, p):
                r = act.value_load(tile_i[0:1, 0, ds(t, 1)], min_val=0, max_val=XROWS - P)
                act.dma_start(xg[p][:, :], rows_dram[ds(r, P), :]).then_inc(row_in[p], 16)

            act.wait_ge(tables_ready, 1)
            act.wait_ge(rows_out, 16 * 2 * NT)
            act.wait_ge(pads_out, 16 * (E + 1))
            load_rows(0, 0)
            load_rows(1, 1)

            def copy_xt(t, p, first=False):
                act.wait_ge(tx_mm, t + 1)
                if not first:
                    act.wait_ge(up_mm, t * 4 - 4)
                nc.scalar.activation(xTs[p][:, :, :], ps[7][:, 0:D].rearrange("p (c t) -> p c t", c=DC),
                                     ACT.Copy).then_inc(tx_ready, 1)

            def silu_up(t, p, first=False):
                for j in range(2):
                    act.wait_ge(up_mm, t * 4 + (2 * j + 1))
                    if not first:
                        act.wait_ge(g_ready, t * 2 + (j - 1))
                    nc.scalar.activation(act_t[:, j * 512:(j + 1) * 512], ps[2 * j][:, :],
                                         ACT.Silu).then_inc(silu_ready, 1)

            def copy_gt(t, p, first=False):
                act.wait_ge(gt_mm, t * 2 + 1)
                if not first:
                    act.wait_ge(tile_mm, t + 1)
                nc.scalar.activation(gT[:, 0:4, :], ps[4][:, :].rearrange("p (j t) -> p j t", t=P),
                                     ACT.Copy).then_inc(gt_a, 1)

            copy_xt(0, 0, True)
            silu_up(0, 0, True)
            copy_xt(1, 1, True)

            def step(t, p, load=True):
                silu_up(t, p)
                if load:
                    act.wait_ge(meta_ready, t)
                    load_rows(t + 1, 1 - p)
                    copy_xt(t + 1, 1 - p)
                copy_gt(t - 1, 1 - p, first=False)

            act.wait_ge(meta_ready, 1)
            act.wait_ge(tx_mm, 1)
            silu_up(1, 1)
            load_rows(2, 0)
            copy_xt(2, 0)
            copy_gt(0, 0, True)
            with act.Fori(1, TILES // 2 - 1) as it:
                for p in range(2):
                    step(it * 2 + p, p)
            step(TILES - 2, 0)
            step(TILES - 1, 1, load=False)
            copy_gt(TILES - 1, 1)

        @block.vector
        def _(dve):
            steps = [0]

            def then(ins):
                steps[0] += 1
                ins.then_inc(dve_step, 1)
                dve.wait_ge(dve_step, steps[0])

            nc.vector.memset(eps_sb[:, :], EPS)
            nc.vector.memset(ones[:, :], 1.0)
            nc.vector.memset(yT[:, :, NG * GT:NP], 0.0).then_inc(zeros_ready, 1)
            with dve.Fori(0, NT // 2) as it:
                for p in range(2):
                    dve.wait_ge(h_ready, it * 2 + (p + 1))
                    nc.vector.bn_stats(stats[:, 0, ds(it * 2 + p, 1), :].rearrange("p a s -> p (a s)"),
                                       h_all[:, ds(it * 2 + p, 1), :].rearrange("p a d -> p (a d)")).then_inc(stat1, 1)

            def inverse_root(k, done, count):
                dve.wait_ge(done, count)
                for t in range(NT):
                    nc.vector.bn_aggr(mv[:, k, t, :], stats[:, k, t, :]).then_inc(mv_ready[k], 1)
                dve.wait_ge(std_ready[k], 1)
                then(nc.vector.reciprocal(rstd[:, k, 1, :], rstd[:, k, 0, :]))

            inverse_root(0, stat1, NT)

            def norm(k, dst, src, t):
                return nc.vector.tensor_scalar(dst, src, mv[:, k, ds(t, 1), 0], rstd[:, k, 1, ds(t, 1)],
                                               ALU.subtract, ALU.mult)

            def row(x, t):
                return x[:, ds(t, 1), :].rearrange("p a d -> p (a d)")

            for p in range(2):
                norm(0, xn[p][:, :], row(h_all, p), p).then_inc(xn_ready, 1)
            with dve.Fori(1, NT // 2) as it:
                for p in range(2):
                    dve.wait_ge(xt_mm, it * 2 + (p - 1))
                    norm(0, xn[p][:, :], row(h_all, it * 2 + p), it * 2 + p).then_inc(xn_ready, 1)
            dve.wait_ge(const_in, ALL_CONST)
            dve.wait_ge(uqk_ready, 6 * (NT // 2))

            def spread_q(g_, half, first):
                if not first:
                    dve.wait_ge(score_mm, g_ * 2 + (half - 1))
                src = qT[:, half, ds(g_ * GT, GT)].rearrange("p (b s) -> p b s", b=GB)
                nc.vector.tensor_tensor(qblk[half][:, :, :, :], src.unsqueeze(2).broadcast_to([P, GB, HH, S]),
                                        mask_sb[:, :].unsqueeze(1).unsqueeze(3).broadcast_to([P, GB, HH, S]),
                                        ALU.mult).then_inc(qblk_ready, 1)

            def gate(g_, half):
                dve.wait_ge(av_mm, g_ * 2 + (half + 1))
                for odd in (1, 0):
                    if not odd:
                        dve.wait_ge(odd_done, g_ * 2 + (half + 1))
                    for r in range(4):
                        lo, n = 32 * r, (32 if odd else 16)
                        col = (2 * r + odd) * S
                        last = nc.vector.scalar_tensor_tensor(
                            yT[lo:lo + n, half, ds(g_ * GT, GT)].rearrange("p (b s) -> p b s", b=GB),
                            av_ps[half][lo:lo + n, :, col:col + S], 1.0 / S,
                            uT[lo:lo + n, half, ds(g_ * GT, GT)].rearrange("p (b s) -> p b s", b=GB),
                            ALU.mult, ALU.mult)
                    last.then_inc(odd_done if odd else y_done, 1)

            for half in range(2):
                spread_q(0, half, True)
            with dve.Fori(1, NG) as gi:
                for half in range(2):
                    spread_q(gi, half, False)
                for half in range(2):
                    gate(gi - 1, half)
            for half in range(2):
                gate(NG - 1, half)

            with dve.Fori(0, NT // 2) as it:
                for p in range(2):
                    dve.wait_ge(ynat_ready, it * 2 + (p + 1))
                    nc.vector.bn_stats(row(stats[:, 1], it * 2 + p), row(y_nat, it * 2 + p)).then_inc(stat2, 1)
            inverse_root(1, stat2, NT)

            def residual(t, p):
                dve.wait_ge(out_mm, t + 1)
                nc.vector.tensor_tensor(row(h_all, t), row(h_all, t), ps[2 + p][:, 0:D], ALU.add).then_inc(h2_ready, 1)
                dve.wait_ge(h2_ready, t + 1)
                nc.vector.bn_stats(row(stats[:, 2], t), row(h_all, t)).then_inc(stat1, 1)

            for p in range(2):
                norm(1, xn[p][:, :], row(y_nat, p), p).then_inc(z_ready, 1)
            with dve.Fori(1, NT // 2) as it:
                for p in range(2):
                    dve.wait_ge(zt_mm, it * 2 + (p - 1))
                    norm(1, xn[p][:, :], row(y_nat, it * 2 + p), it * 2 + p).then_inc(z_ready, 1)
                for p in range(2):
                    residual(it * 2 + (p - 2), p)
            for p in range(2):
                residual(NT - 2 + p, p)
            inverse_root(2, stat1, 2 * NT)

            def logits(t, p):
                dve.wait_ge(lg_mm, t + 1)
                nc.vector.tensor_copy(row(lg, t), ps[2 + p][:, 0:E]).then_inc(lg_ready, 1)

            dve.wait_ge(zt_mm, NT)
            for p in range(2):
                norm(2, xn[p][:, :], row(h_all, p), p).then_inc(hn_ready, 1)
            with dve.Fori(1, NT // 2) as it:
                for p in range(2):
                    dve.wait_ge(hnt_mm, it * 2 + (p - 1))
                    dve.wait_ge(row_ready, it * 2 + (p - 1))
                    norm(2, xn[p][:, :], row(h_all, it * 2 + p), it * 2 + p).then_inc(hn_ready, 1)
                for p in range(2):
                    logits(it * 2 + (p - 2), p)
            for p in range(2):
                logits(NT - 2 + p, p)
            dve.wait_ge(lg_ready, NT)

            def over_e(x):
                return x.unsqueeze(2).broadcast_to([P, NT, E])

            em8 = c8_sb[:, 0, :].unsqueeze(1).broadcast_to([P, NT, E])
            region = c8_sb[:, 1, :].unsqueeze(1).broadcast_to([P, NT, E])

            def top(src, one_hot, value, expert):
                then(nc.vector.tensor_reduce(value, src, AX, ALU.max))
                then(nc.vector.tensor_tensor(r8[:, 0], src, over_e(value), ALU.is_equal))
                then(nc.vector.tensor_tensor(r8[:, 1], r8[:, 0], em8, ALU.mult))
                then(nc.vector.tensor_reduce(expert, r8[:, 1], AX, ALU.min))
                then(nc.vector.tensor_tensor(one_hot, em8, over_e(expert), ALU.is_equal))

            top(lg[:, :, :], r8[:, 2], r1[:, 0, :], r1[:, 1, :])
            then(nc.vector.scalar_tensor_tensor(r8[:, 4], r8[:, 2], -3.0e38, lg[:, :, :], ALU.mult, ALU.add))
            top(r8[:, 4], r8[:, 3], r1[:, 2, :], r1[:, 5, :])
            nc.vector.tensor_tensor(r1[:, 3, :], r1[:, 2, :], r1[:, 0, :], ALU.subtract).then_inc(gap_ready, 1)
            then(nc.vector.tensor_tensor(r8[:, 5], r8[:, 2], r8[:, 3], ALU.add))
            nc.vector.tensor_tensor(r8[:, 6], r8[:, 5], over_e(tokid_sb[:, 1, :]), ALU.mult).then_inc(sel_ready, 1)
            dve.wait_ge(expw_ready, 1)
            then(nc.vector.tensor_scalar(r1[:, 6, :], r1[:, 4, :], 1.0, None, ALU.add))
            then(nc.vector.reciprocal(r1[:, 7, :], r1[:, 6, :]))
            then(nc.vector.tensor_tensor(r1[:, 8, :], r1[:, 4, :], r1[:, 7, :], ALU.mult))
            nc.vector.tensor_copy(rows[:, :, D], tokid_sb[:, 0, :])
            nc.vector.tensor_copy(rows[:, :, D + 1], r1[:, 1, :])
            nc.vector.tensor_copy(rows[:, :, D + 2], r1[:, 8, :])
            then(nc.vector.tensor_tensor(rows[:, :, D + 3], r1[:, 7, :], r1[:, 8, :], ALU.subtract))
            dve.wait_ge(rank_mm, 1)
            then(nc.vector.tensor_copy(r8[:, 7], ps[5][:, 0:NT * E].rearrange("p (t e) -> p t e", e=E)))
            then(nc.vector.memset(r8[:, 8, 0, :], 0.0))
            for t in range(1, NT):
                then(nc.vector.tensor_tensor(r8[:, 8, t, :], r8[:, 8, t - 1, :], r8[:, 7, t - 1, :], ALU.add))
            then(nc.vector.tensor_tensor(e8[:, 0, :], r8[:, 8, NT - 1, :], r8[:, 7, NT - 1, :], ALU.add))
            then(nc.vector.tensor_tensor(r8[:, 9], ps[4][:, 0:NT * E].rearrange("p (t e) -> p t e", e=E), r8[:, 8], ALU.add))
            then(nc.vector.tensor_tensor(r8[:, 1], r8[:, 9], region, ALU.add))
            for c in range(2):
                then(nc.vector.tensor_tensor(r8[:, 0], r8[:, 1], r8[:, 2 + c], ALU.mult))
                then(nc.vector.tensor_reduce(r1[:, 9, :], r8[:, 0], AX, ALU.add))
                then(nc.vector.tensor_copy(slot_i[:, c, :], r1[:, 9, :]))
            nc.vector.tensor_copy(slot_i[:, 1, :], r1[:, 9, :]).then_inc(slots_ready, 1)
            then(nc.vector.tensor_tensor(e8[:, 1, :], e8[:, 0, :], c8_sb[:, 1, :], ALU.add))
            then(nc.vector.tensor_copy(exp_i[:, 0, :], e8[:, 1, :]))
            by_slot = r8[:, 0].rearrange("p t e -> p (t e)").rearrange("p (e t) -> p e t", e=E)
            then(nc.vector.tensor_tensor(by_slot, e8[:, 0, :].unsqueeze(2).broadcast_to([P, E, NT]),
                                         cslot_sb[:, :].unsqueeze(1).broadcast_to([P, E, NT]), ALU.is_gt))
            then(nc.vector.tensor_reduce(e8[:, 2, :], by_slot, AX, ALU.add))
            then(nc.vector.tensor_copy(e8[:, 3, 0:1], e8[:, 2, 0:1]))
            for e in range(1, E):
                then(nc.vector.tensor_tensor(e8[:, 3, e:e + 1], e8[:, 3, e - 1:e], e8[:, 2, e:e + 1], ALU.add))
            then(nc.vector.tensor_scalar(e8[:, 4, :], e8[:, 3, :], 1.0, None, ALU.add))
            then(nc.vector.tensor_copy(exp_i[:, 1, :], e8[:, 4, :]))
            ends = e8[:, 3, :].unsqueeze(1).broadcast_to([P, TILES, E])
            tiles = ctile_sb[:, :].unsqueeze(2).broadcast_to([P, TILES, E])
            then(nc.vector.tensor_tensor(te[:, 0], ends, tiles, ALU.is_le))
            then(nc.vector.tensor_reduce(t1[:, 0, :], te[:, 0], AX, ALU.add))
            then(nc.vector.tensor_tensor(te[:, 1], te[:, 0], ends, ALU.mult))
            then(nc.vector.tensor_reduce(t1[:, 1, :], te[:, 1], AX, ALU.max))
            then(nc.vector.tensor_tensor(t1[:, 2, :], ctile_sb[:, :], t1[:, 1, :], ALU.subtract))
            then(nc.vector.tensor_scalar(t1[:, 3, :], t1[:, 0, :], float(E), float(P), ALU.is_lt, ALU.mult))
            then(nc.vector.tensor_tensor(t1[:, 4, :], t1[:, 2, :], t1[:, 3, :], ALU.mult))
            then(nc.vector.scalar_tensor_tensor(t1[:, 5, :], t1[:, 0, :], float(CAP), t1[:, 4, :], ALU.mult, ALU.add))
            then(nc.vector.tensor_copy(tile_i[:, 0, :], t1[:, 5, :]))
            then(nc.vector.tensor_scalar(t1[:, 6, :], t1[:, 0, :], -float(E), None, ALU.add))
            then(nc.vector.tensor_scalar(t1[:, 7, :], t1[:, 0, :], float(E - 1), None, ALU.min))
            then(nc.vector.tensor_scalar(t1[:, 8, :], t1[:, 7, :], 1.0, 16.0, ALU.add, ALU.mult))
            then(nc.vector.tensor_copy(tile_i[:, 2, :], t1[:, 8, :]))
            for m in range(RING, E, RING):
                then(nc.vector.tensor_scalar(t1[:, 9, :], t1[:, 7, :], float(RING), -float(RING), ALU.is_ge, ALU.mult))
                then(nc.vector.tensor_tensor(t1[:, 7, :], t1[:, 7, :], t1[:, 9, :], ALU.add))
            nc.vector.tensor_copy(tile_i[:, 1, :], t1[:, 7, :]).then_inc(tables_ready, 1)

            def meta(t, p, first=False):
                dve.wait_ge(row_in[p], (t - p) * 8 + 16)
                if not first:
                    dve.wait_ge(added, t * 16 - 16)
                then_meta(nc.vector.tensor_scalar(wt[p][:, 0:1], xg[p][:, D + 1:D + 2], t1[:, 6, ds(t, 1)],
                                                  xg[p][:, D + 3:D + 4], ALU.is_equal, ALU.mult), t, 0)
                then_meta(nc.vector.tensor_tensor(wt[p][:, 1:2], wt[p][:, 0:1], xg[p][:, D + 2:D + 3], ALU.add), t, 1)
                dve.wait_ge(tx_mm, t + 1)
                nc.vector.tensor_copy(tok_i[p][:, :], xg[p][:, D:D + 1]).then_inc(meta_ready, 1)

            base = steps[0]

            def then_meta(ins, t, k):
                ins.then_inc(dve_step, 1)
                dve.wait_ge(dve_step, t * 2 + (base + k + 1))

            def gated(t, p, first=False):
                for j in range(2):
                    dve.wait_ge(silu_ready, t * 2 + (j + 1))
                    dve.wait_ge(up_mm, t * 4 + (2 * j + 2))
                    if not first:
                        dve.wait_ge(gt_mm, t * 2 - 2)
                    nc.vector.tensor_tensor(g[p][:, j * 512:(j + 1) * 512], act_t[:, j * 512:(j + 1) * 512],
                                            ps[2 * j + 1][:, :], ALU.mult).then_inc(g_ready, 1)

            def copy_gt(t, p, first=False):
                dve.wait_ge(gt_mm, t * 2 + 2)
                if not first:
                    dve.wait_ge(tile_mm, t + 1)
                nc.vector.tensor_copy(gT[:, 4:8, :], ps[5][:, :].rearrange("p (j t) -> p j t", t=P)).then_inc(gt_b, 1)

            def weigh(t, p):
                dve.wait_ge(tile_mm, t + 2)
                nc.vector.tensor_scalar(ysb[p][:, :], ps[6][:, 0:D], wt[p][:, 1:2], None, ALU.mult).then_inc(y_ready, 1)

            meta(0, 0, True)
            gated(0, 0, True)

            def step(t, p, second=False):
                meta(t, p, second)
                gated(t, p, second)
                copy_gt(t - 1, 1 - p, second)
                weigh(t - 1, 1 - p)

            step(1, 1, True)
            with dve.Fori(1, TILES // 2) as it:
                for p in range(2):
                    step(it * 2 + p, p)
            copy_gt(TILES - 1, 1)
            weigh(TILES - 1, 1)

        @block.tensor
        def _(pe):
            mm = nc.tensor.matmul

            pe.wait_ge(embed_w_in, 32)

            def embed(it, p, first):
                pe.wait_ge(x_in[p], it * 32 + 32)
                if not first:
                    pe.wait_ge(h_ready, it * 2 + (p - 1))
                for c in range(KC):
                    mm(ps[p][:, 0:D], xb[p][:, c, :], wemb_sb[:, c, :], start=(c == 0), stop=False)
                mm(ps[p][:, 0:D], pb[p][:, :], wpos_sb[:, :], start=False, stop=True).then_inc(embed_mm, 1)

            for p in range(2):
                embed(0, p, True)
            with pe.Fori(1, NT // 2) as it:
                for p in range(2):
                    embed(it, p, False)

            def flip(dst, src):
                for c in range(DC):
                    last = nc.tensor.transpose(dst[:, c * P:(c + 1) * P], src[:, c * P:(c + 1) * P], ident[:, :])
                return last

            pe.wait_ge(ident_ready, 1)
            pe.wait_ge(zeros_ready, 1)
            pe.wait_ge(const_in, ALL_CONST)
            pe.wait_ge(h_ready, NT)

            def flip_xn(it, first):
                for p in range(2):
                    pe.wait_ge(xn_ready, it * 2 + (p + 1))
                    if not first:
                        pe.wait_ge(xt_ready, it * 2 + (p - 1))
                    flip(ps[p], xn[p]).then_inc(xt_mm, 1)

            def project(it, first):
                pe.wait_ge(xt_ready, it * 2 + 2)
                for f in range(6):
                    col = (0, 2, 3)[f // 2] * D + (f % 2) * P
                    if not first:
                        pe.wait_ge(uqk_ready, (it - 1) * 6 + (2 * (f // 2) + 2))
                    for c in range(DC):
                        last = mm(ps[2 + f // 2][:, (f % 2) * 256:(f % 2) * 256 + 256], w1_sb[:, c, col:col + P],
                                  xT[:, c, :], start=(c == 0), stop=(c == DC - 1))
                    last.then_inc(proj_mm, 1)
                if not first:
                    pe.wait_ge(v_ready, it * 2)
                for p in range(2):
                    dst = ps[5][:, p * 256:p * 256 + 256]
                    for c in range(DC):
                        mm(dst, xT[:, c, p * P:(p + 1) * P], w1_sb[:, c, D:2 * D], start=(c == 0), stop=False)
                    mm(dst, ones[0:1, :], b1v_sb[:, :], start=False, stop=True).then_inc(v_mm, 1)

            flip_xn(0, True)
            project(0, True)
            with pe.Fori(1, NT // 2) as it:
                flip_xn(it, False)
                project(it, False)

            pe.wait_ge(v_ready, NT)
            pe.wait_ge(uqk_ready, 6 * (NT // 2))

            def scores(g_, half, first):
                pe.wait_ge(qblk_ready, g_ * 2 + (half + 1))
                pe.wait_ge(kz_ready, g_ * 2 + (half + 1))
                if not first:
                    pe.wait_ge(at_ready, g_ * 2 + (half - 1))
                for b in range(GB):
                    last = mm(ps[half][0:GT, 0:HH * S], kz[half][:, b * GT:(b + 1) * GT],
                              qblk[half][:, b, :, :], start=(b == 0), stop=(b == GB - 1))
                last.then_inc(score_mm, 1)

            def values(g_, half, first):
                pe.wait_ge(at_ready, g_ * 2 + (half + 1))
                pe.wait_ge(vz_in[half], g_ * (16 * GB) + 16 * GB)
                if not first:
                    pe.wait_ge(y_done, g_ * 2 + (half - 1))
                for b in range(GB):
                    last = mm(av_ps[half][:, b, 0:HH * S], vz[half][0:GT, b, :], at[half][:, :],
                              start=True, stop=True)
                last.then_inc(av_mm, 1)

            def group(g_, first):
                for half in range(2):
                    scores(g_, half, first)
                for half in range(2):
                    values(g_, half, first)

            group(0, True)
            with pe.Fori(1, NG) as gi:
                group(gi, False)

            def flip_y(it, p, first):
                pe.wait_ge(ycur_ready, it * 2 + (p + 1))
                if not first:
                    pe.wait_ge(ynat_ready, it * 2 + (p - 1))
                flip(ps[p], ycur[p][:, :, :].rearrange("p c t -> p (c t)")).then_inc(yt_mm, 1)

            for p in range(2):
                flip_y(0, p, True)
            with pe.Fori(1, NT // 2) as it:
                for p in range(2):
                    flip_y(it, p, False)
            pe.wait_ge(ynat_ready, NT)

            def flip_z(it, p, first):
                pe.wait_ge(z_ready, it * 2 + (p + 1))
                if not first:
                    pe.wait_ge(zt_ready, it * 2 + (p - 1))
                flip(ps[p], xn[p]).then_inc(zt_mm, 1)

            def out_proj(it, p, first):
                pe.wait_ge(zt_ready, it * 2 + (p + 1))
                if not first:
                    pe.wait_ge(h2_ready, it * 2 + (p - 1))
                for c in range(DC):
                    mm(ps[2 + p][:, 0:D], zT[p][:, c, :], w2_sb[:, c, :], start=(c == 0), stop=False)
                mm(ps[2 + p][:, 0:D], ones[0:1, :], b2_sb[:, :], start=False, stop=True).then_inc(out_mm, 1)

            pe.wait_ge(y_done, 2 * NG)
            for p in range(2):
                flip_z(0, p, True)
            for p in range(2):
                out_proj(0, p, True)
            with pe.Fori(1, NT // 2) as it:
                for p in range(2):
                    flip_z(it, p, False)
                for p in range(2):
                    out_proj(it, p, False)
            pe.wait_ge(h2_ready, NT)

            def flip_hn(it, p, first):
                pe.wait_ge(hn_ready, it * 2 + (p + 1))
                if not first:
                    pe.wait_ge(hnt_ready, it * 2 + (p - 1))
                flip(ps[p], xn[p]).then_inc(hnt_mm, 1)

            def logits(it, p, first):
                pe.wait_ge(hnt_ready, it * 2 + (p + 1))
                if not first:
                    pe.wait_ge(lg_ready, it * 2 + (p - 1))
                for c in range(DC):
                    last = mm(ps[2 + p][:, 0:E], zT[p][:, c, :], wg_sb[:, c, :], start=(c == 0), stop=(c == DC - 1))
                last.then_inc(lg_mm, 1)

            for p in range(2):
                flip_hn(0, p, True)
            for p in range(2):
                logits(0, p, True)
            with pe.Fori(1, NT // 2) as it:
                for p in range(2):
                    flip_hn(it, p, False)
                for p in range(2):
                    logits(it, p, False)
            pe.wait_ge(sel_ready, 1)
            sel = r8[:, 6].rearrange("p t e -> p (t e)")
            mm(ps[4][:, 0:NT * E], tri_sb[:, :], sel, start=True, stop=True).then_inc(tile_mm, 1)
            mm(ps[5][:, 0:NT * E], ones[:, :], sel, start=True, stop=True).then_inc(rank_mm, 1)

            pe.wait_ge(tables_ready, 1)
            pe.wait_ge(w_in, 16 * RING)

            def flip_x(t, p, first=False):
                pe.wait_ge(row_in[p], (t - p) * 8 + 16)
                if not first:
                    pe.wait_ge(tx_ready, t)
                flip(ps[7], xg[p]).then_inc(tx_mm, 1)

            def up(t, p, first=False):
                r = pe.value_load(tile_i[0:1, 2, ds(t, 1)], min_val=16, max_val=16 * E)
                s = pe.value_load(tile_i[0:1, 1, ds(t, 1)], min_val=0, max_val=RING - 1)
                pe.wait_ge(w_in, r)
                pe.wait_ge(tx_ready, t + 1)
                for j in range(2):
                    for k in range(2):
                        if not first:
                            pe.wait_ge(g_ready if k else silu_ready, t * 2 + (j - 1))
                        for c in range(DC):
                            o = k * W1C + c * F + j * 512
                            last = mm(ps[2 * j + k][:, :], xTs[p][:, c, :], ring[:, s, o:o + 512],
                                      start=(c == 0), stop=(c == DC - 1))
                        last.then_inc(up_mm, 1)
                return s

            def down(t, p, first=False):
                s = pe.value_load(tile_i[0:1, 1, ds(t, 1)], min_val=0, max_val=RING - 1)
                for j in range(2):
                    pe.wait_ge(g_ready, t * 2 + (j + 1))
                    if not first:
                        pe.wait_ge(gt_b if j else gt_a, t)
                    for i in range(4):
                        last = nc.tensor.transpose(ps[4 + j][:, i * P:(i + 1) * P],
                                                   g[p][:, (4 * j + i) * P:(4 * j + i + 1) * P], ident[:, :])
                    last.then_inc(gt_mm, 1)
                if not first:
                    pe.wait_ge(y_ready, t)
                for i in range(8):
                    if i % 4 == 0:
                        pe.wait_ge(gt_b if i else gt_a, t + 1)
                    o = W1C + W3C + i * D
                    last = mm(ps[6][:, 0:D], gT[:, i, :], ring[:, s, o:o + D], start=(i == 0), stop=(i == 7))
                last.then_inc(tile_mm, 1)

            flip_x(0, 0, True)
            up(0, 0, True)
            flip_x(1, 1)
            up(1, 1)
            flip_x(2, 0)
            down(0, 0, True)
            with pe.Fori(1, TILES // 2 - 1) as it:
                for p in range(2):
                    t = it * 2 + p
                    up(t, p)
                    flip_x(t + 1, 1 - p)
                    down(t - 1, 1 - p)
            up(TILES - 2, 0)
            flip_x(TILES - 1, 1)
            down(TILES - 3, 1)
            up(TILES - 1, 1)
            down(TILES - 2, 0)
            down(TILES - 1, 1)


def kernel(**inputs):
    import numpy as np
    import concourse.bacc as bacc
    from concourse.bass_utils import run_bass_kernel_spmd

    a = {k: np.asarray(v) for k, v in inputs.items()}
    f = np.float32

    def chunks(w):
        return w.reshape(-1, P, w.shape[1]).transpose(1, 0, 2)

    x = a["x"].reshape(B, C, NPH, PATCH, NPH, PATCH).transpose(0, 2, 4, 1, 3, 5).reshape(B, S - 1, PD)
    tok = np.zeros((NP, PD), x.dtype)
    tok[:N].reshape(B, S, PD)[:, 1:] = x
    xpatch = tok.reshape(NT, P, KC, P).transpose(0, 3, 2, 1)
    hot = np.zeros((NP, NPOS), f)
    n = np.arange(N)
    hot[n, n % S] = 1
    hot[n, np.where(n % S == 0, S + 1, S)] = 1
    onehot = hot.reshape(NT, P, NPOS).transpose(0, 2, 1)
    wpos = np.concatenate([a["L0_tok_pos_embed"][0], a["L0_tok_b"][None], a["L0_tok_cls_token"][0]], 0)
    b1 = a["L0_attn_b1"].reshape(4, DC, P)
    e1 = a["L0_ffn_W1"].reshape(E, DC, P, F).transpose(0, 2, 1, 3).reshape(E, P, W1C)
    e3 = a["L0_ffn_W3"].reshape(E, DC, P, F).transpose(0, 2, 1, 3).reshape(E, P, W3C)
    e2 = a["L0_ffn_W2"].reshape(E, F // P, P, D).transpose(0, 2, 1, 3).reshape(E, P, W2C)

    def wide(v):
        return np.broadcast_to(np.asarray(v, f), (P,) + np.shape(v))

    token = np.arange(NP).reshape(NT, P).T
    pad = np.zeros((P, ROW), f)
    pad[:, D] = N + np.arange(P)
    arrays = {
        "xpatch": xpatch, "onehot": onehot, "wemb": chunks(a["L0_tok_W"].T), "wpos": wpos,
        "w1": chunks(a["L0_attn_W1"]), "b1f": b1[[0, 2, 3]].reshape(6, P).T, "b1v": b1[1].reshape(1, D),
        "w2": chunks(a["L0_attn_W2"]), "b2": a["L0_attn_b2"].reshape(1, D),
        "gamma": a["L0_attn_gamma"].reshape(DC, P).T, "beta": a["L0_attn_beta"].reshape(DC, P).T,
        "wg": chunks(a["L0_ffn_Wg"]), "experts": np.concatenate([e1, e3, e2], 2),
        "headmask": (np.arange(P)[:, None] // DH == np.arange(HH)).astype(f),
        "c8": wide([np.arange(E) - E, np.arange(E) * CAP]), "ctile": wide(np.arange(TILES)),
        "cslot": wide(np.arange(NT) * P),
        "tokid": np.stack([token, token < N], 1).astype(f),
        "tri": (np.arange(P)[:, None] < np.arange(P)).astype(f), "padrow": pad,
    }
    nc = bacc.Bacc("TRN2", target_bir_lowering=False, num_devices=1)
    feeds, args = {}, {}
    for name, v in arrays.items():
        v = np.ascontiguousarray(v)
        feeds[f"in_{name}"] = v
        args[name] = nc.dram_tensor(f"in_{name}", v.shape, mybir.dt.from_np(v.dtype), kind="ExternalInput").ap()
    args["out"] = nc.dram_tensor("out_0", [N + P, D], mybir.dt.float32, kind="ExternalOutput").ap()
    vit_block_kernel(nc, **args)
    r = run_bass_kernel_spmd(nc, [feeds], core_ids=[0])
    return r.results[0]["out_0"][:N].reshape(B, S, D)
```
